# Optimizing a Trainium2 kernel written in Bass

```python
import numpy as np
import jax
import jax.numpy as jnp

def _softmax(x, axis=-1):
    return jax.nn.softmax(x, axis=axis)

def _gelu(x):
    return jax.nn.gelu(x, approximate=True)

def _silu(x):
    return jax.nn.silu(x)

def _sigmoid(x):
    return jax.nn.sigmoid(x)

def _layernorm(x, axis=-1, eps=1e-05):
    m = jnp.mean(x, axis=axis, keepdims=True)
    v = jnp.var(x, axis=axis, keepdims=True)
    return (x - m) / jnp.sqrt(v + eps)

def _scatter_add(tgt, idx, src, axis=0):
    return tgt.at[idx].add(src)

def _segment_sum(src, seg, n):
    return jax.ops.segment_sum(src, seg, n)
kernel_name = 'mk_adj_resnorm_d4_adj_r2_0f46ea'

def setup_inputs(seed: int=0):
    np.random.seed(seed)
    _w = jnp.asarray

    def _rec_inputs():
        import jax
        import jax.numpy as jnp
        _gk = jax.random.key(seed)
        x = -0.0003929 + 0.9999 * jax.random.normal(jax.random.fold_in(_gk, 1), (32, 256, 128), jnp.float32)
        _a = jax.random.bernoulli(jax.random.fold_in(_gk, 2), 0.015625, (256, 256))
        _a = jnp.logical_or(_a, jnp.swapaxes(_a, -1, -2))
        _a = jnp.logical_or(_a, jnp.eye(256, dtype=bool))
        _af = _a.astype(jnp.float32)
        _af = _af / jnp.maximum(_af.sum(-1, keepdims=True), 1.0)
        adj = _af
        return (x, adj)
    x, adj = _rec_inputs()

    def _L0_gnn_setup():
        import jax, jax.numpy as jnp
        import numpy as np
        B, N, D = (128, 256, 128)

        def _make_adj(k):
            a = jax.random.uniform(k, (N, N), dtype=jnp.float32)
            mask = (jax.random.uniform(jax.random.fold_in(k, 1), (N, N)) < 4.0 / N).astype(jnp.float32)
            a = a * mask
            return a / (a.sum(axis=1, keepdims=True) + 1e-08)
        key = jax.random.key(seed)
        ks = jax.random.split(key, 8)
        x = jax.random.normal(ks[0], (B, N, D), dtype=jnp.float32)
        adj_in = _make_adj(ks[1])
        adj_out = _make_adj(ks[2])
        bias_in = jax.random.normal(ks[3], (N, D), dtype=jnp.float32) * 0.02
        bias_out = jax.random.normal(ks[4], (N, D), dtype=jnp.float32) * 0.02
        gate_w_in = jax.random.normal(ks[5], (D, 1), dtype=jnp.float32) * 0.02
        gate_b_in = jnp.zeros((N, 1), dtype=jnp.float32)
        gate_w_out = jax.random.normal(ks[6], (D, 1), dtype=jnp.float32) * 0.02
        gate_b_out = jnp.zeros((N, 1), dtype=jnp.float32)
        loop_gate = jax.random.normal(ks[7], (D, 1), dtype=jnp.float32) * 0.02
        return {'x': x, 'adj_in': adj_in, 'adj_out': adj_out, 'bias_in': bias_in, 'bias_out': bias_out, 'gate_w_in': gate_w_in, 'gate_b_in': gate_b_in, 'gate_w_out': gate_w_out, 'gate_b_out': gate_b_out, 'loop_gate': loop_gate}
    _L0_gnn_all = _L0_gnn_setup()
    _L0_gnn_in = {k: v for k, v in _L0_gnn_all.items() if k in ('bias_in', 'bias_out', 'gate_w_in', 'gate_b_in', 'gate_w_out', 'gate_b_out', 'loop_gate')}
    del _L0_gnn_all

    def _L1_gnn_setup():
        import jax, jax.numpy as jnp
        import numpy as np
        EPS = 1e-05

        def _batchnorm(x, gamma, beta):
            mu = jnp.mean(x, axis=0)
            var = jnp.var(x, axis=0)
            return (x - mu) * jax.lax.rsqrt(var + EPS) * gamma + beta
        key = jax.random.key(seed)
        ks = jax.random.split(key, 4)
        b, n, d, h, o = (32, 1024, 128, 256, 128)
        features = jax.random.normal(ks[0], (b, n, d), dtype=jnp.float32)
        A = jax.random.uniform(ks[1], (n, n), dtype=jnp.float32)
        lim1 = float(np.sqrt(6.0 / (d + h)))
        W1 = jax.random.uniform(ks[2], (h, d), minval=-lim1, maxval=lim1, dtype=jnp.float32)
        b1 = jnp.zeros((h,), jnp.float32)
        lim2 = float(np.sqrt(6.0 / (h + o)))
        W2 = jax.random.uniform(ks[3], (o, h), minval=-lim2, maxval=lim2, dtype=jnp.float32)
        b2 = jnp.zeros((o,), jnp.float32)
        g1 = jnp.ones((h,), jnp.float32)
        be1 = jnp.zeros((h,), jnp.float32)
        g2 = jnp.ones((o,), jnp.float32)
        be2 = jnp.zeros((o,), jnp.float32)
        return {'features': features, 'A': A, 'W1': W1, 'b1': b1, 'g1': g1, 'be1': be1, 'W2': W2, 'b2': b2, 'g2': g2, 'be2': be2}
    _L1_gnn_all = _L1_gnn_setup()
    _L1_gnn_in = {k: v for k, v in _L1_gnn_all.items() if k in ('W1', 'b1', 'g1', 'be1', 'W2', 'b2', 'g2', 'be2')}
    del _L1_gnn_all

    def _L2_gnn_setup():
        import jax, jax.numpy as jnp
        import numpy as np
        ALPHA = 0.2
        key = jax.random.key(seed)
        k1, k2, k3, k4 = jax.random.split(key, 4)
        B, N, Fin, Fout = (8, 1024, 128, 128)
        h = jax.random.normal(k1, (B, N, Fin), dtype=jnp.float32)
        adj = jax.random.randint(k2, (N, N), 0, 2).astype(jnp.float32)
        adj = jnp.maximum(adj, jnp.eye(N, dtype=jnp.float32))

        def xavier(k, shape, gain=1.414):
            fan_in, fan_out = (shape[0], shape[1])
            a = gain * np.sqrt(6.0 / (fan_in + fan_out))
            return jax.random.uniform(k, shape, dtype=jnp.float32, minval=-a, maxval=a)
        W = xavier(k3, (Fin, Fout))
        a = xavier(k4, (2 * Fout, 1))
        return {'h': h, 'adj_matrix': adj, 'W': W, 'a': a}
    _L2_gnn_all = _L2_gnn_setup()
    _L2_gnn_in = {k: v for k, v in _L2_gnn_all.items() if k in ('W', 'a')}
    del _L2_gnn_all

    def _L3_gnn_setup():
        import jax, jax.numpy as jnp
        import numpy as np
        B, T, D, H = (64, 1024, 128, 128)
        MAX_SKIP = 4

        def _lstm_last(Wih, Whh, bih, bhh, xs):
            N, _, Hd = xs.shape
            bias = bih + bhh

            def step(carry, x_t):
                h, c = carry
                g = x_t @ Wih.T + h @ Whh.T + bias
                i, f, gg, o = jnp.split(g, 4, axis=-1)
                c = jax.nn.sigmoid(f) * c + jax.nn.sigmoid(i) * jnp.tanh(gg)
                h = jax.nn.sigmoid(o) * jnp.tanh(c)
                return ((h, c), None)
            init = (jnp.zeros((N, Hd), xs.dtype), jnp.zeros((N, Hd), xs.dtype))
            (h_last, _), _ = jax.lax.scan(step, init, jnp.swapaxes(xs, 0, 1))
            return h_last
        key = jax.random.key(seed)
        ks = jax.random.split(key, 8)
        s = 0.05
        x = jax.random.normal(ks[0], (B, T, D), jnp.float32)
        adj = jax.random.uniform(ks[1], (T, T), jnp.float32) / T
        Wg0 = jax.random.normal(ks[2], (D, H), jnp.float32) * s
        bg0 = jnp.zeros((H,), jnp.float32)
        Wg1 = jax.random.normal(ks[3], (H, H), jnp.float32) * s
        bg1 = jnp.zeros((H,), jnp.float32)
        Wih = jax.random.normal(ks[4], (MAX_SKIP, 4 * H, H), jnp.float32) * s
        Whh = jax.random.normal(ks[5], (MAX_SKIP, 4 * H, H), jnp.float32) * s
        bih = jax.random.normal(ks[6], (MAX_SKIP, 4 * H), jnp.float32) * s
        bhh = jax.random.normal(ks[7], (MAX_SKIP, 4 * H), jnp.float32) * s
        return dict(x=x, adj=adj, Wg0=Wg0, bg0=bg0, Wg1=Wg1, bg1=bg1, Wih=Wih, Whh=Whh, bih=bih, bhh=bhh)
    _L3_gnn_all = _L3_gnn_setup()
    _L3_gnn_in = {k: v for k, v in _L3_gnn_all.items() if k in ('Wg0', 'bg0', 'Wg1', 'bg1', 'Wih', 'Whh', 'bih', 'bhh')}
    del _L3_gnn_all
    return {'x': x, 'adj': adj, 'L0_gnn_bias_in': _L0_gnn_in['bias_in'], 'L0_gnn_bias_out': _L0_gnn_in['bias_out'], 'L0_gnn_gate_w_in': _L0_gnn_in['gate_w_in'], 'L0_gnn_gate_b_in': _L0_gnn_in['gate_b_in'], 'L0_gnn_gate_w_out': _L0_gnn_in['gate_w_out'], 'L0_gnn_gate_b_out': _L0_gnn_in['gate_b_out'], 'L0_gnn_loop_gate': _L0_gnn_in['loop_gate'], 'L1_gnn_W1': _L1_gnn_in['W1'], 'L1_gnn_b1': _L1_gnn_in['b1'], 'L1_gnn_g1': _L1_gnn_in['g1'], 'L1_gnn_be1': _L1_gnn_in['be1'], 'L1_gnn_W2': _L1_gnn_in['W2'], 'L1_gnn_b2': _L1_gnn_in['b2'], 'L1_gnn_g2': _L1_gnn_in['g2'], 'L1_gnn_be2': _L1_gnn_in['be2'], 'L2_gnn_W': _L2_gnn_in['W'], 'L2_gnn_a': _L2_gnn_in['a'], 'L3_gnn_Wg0': _L3_gnn_in['Wg0'], 'L3_gnn_bg0': _L3_gnn_in['bg0'], 'L3_gnn_Wg1': _L3_gnn_in['Wg1'], 'L3_gnn_bg1': _L3_gnn_in['bg1'], 'L3_gnn_Wih': _L3_gnn_in['Wih'], 'L3_gnn_Whh': _L3_gnn_in['Whh'], 'L3_gnn_bih': _L3_gnn_in['bih'], 'L3_gnn_bhh': _L3_gnn_in['bhh']}

def reference(x, adj, L0_gnn_bias_in, L0_gnn_bias_out, L0_gnn_gate_w_in, L0_gnn_gate_b_in, L0_gnn_gate_w_out, L0_gnn_gate_b_out, L0_gnn_loop_gate, L1_gnn_W1, L1_gnn_b1, L1_gnn_g1, L1_gnn_be1, L1_gnn_W2, L1_gnn_b2, L1_gnn_g2, L1_gnn_be2, L2_gnn_W, L2_gnn_a, L3_gnn_Wg0, L3_gnn_bg0, L3_gnn_Wg1, L3_gnn_bg1, L3_gnn_Wih, L3_gnn_Whh, L3_gnn_bih, L3_gnn_bhh):
    import jax
    import jax.numpy as jnp

    def _L0_gnn_ref(x, adj_in, adj_out, bias_in, bias_out, gate_w_in, gate_b_in, gate_w_out, gate_b_out, loop_gate):
        import jax, jax.numpy as jnp
        import numpy as np
        B, N, D = (128, 256, 128)

        def _make_adj(k):
            a = jax.random.uniform(k, (N, N), dtype=jnp.float32)
            mask = (jax.random.uniform(jax.random.fold_in(k, 1), (N, N)) < 4.0 / N).astype(jnp.float32)
            a = a * mask
            return a / (a.sum(axis=1, keepdims=True) + 1e-08)
        msg_in = (jnp.einsum('nm,bmd->bnd', adj_in, x) + bias_in) * jax.nn.sigmoid(x @ gate_w_in + gate_b_in)
        msg_out = (jnp.einsum('nm,bmd->bnd', adj_out, x) + bias_out) * jax.nn.sigmoid(x @ gate_w_out + gate_b_out)
        msg_loop = x * jax.nn.sigmoid(x @ loop_gate)
        return jax.nn.relu(msg_in + msg_out + msg_loop)

    def _L1_gnn_ref(features, A, W1, b1, g1, be1, W2, b2, g2, be2):
        import jax, jax.numpy as jnp
        import numpy as np
        EPS = 1e-05

        def _batchnorm(x, gamma, beta):
            mu = jnp.mean(x, axis=0)
            var = jnp.var(x, axis=0)
            return (x - mu) * jax.lax.rsqrt(var + EPS) * gamma + beta
        b, n, d = features.shape
        A_norm = A + jnp.eye(n, dtype=A.dtype)
        deg = jnp.sum(A_norm, axis=0) + jnp.sum(A_norm, axis=1) - jnp.diagonal(A_norm)
        dinv = jax.lax.rsqrt(deg)
        A_hat = A_norm * dinv[:, None] * dinv[None, :]
        agg = jnp.einsum('nm,bmd->bnd', A_hat, features)
        x = agg.reshape(-1, d)
        h = jax.nn.relu(_batchnorm(x @ W1.T + b1, g1, be1))
        out = h @ W2.T + b2
        out = _batchnorm(out, g2, be2)
        return out.reshape(b, n, -1)

    def _L2_gnn_ref(h, adj_matrix, W, a):
        import jax, jax.numpy as jnp
        import numpy as np
        ALPHA = 0.2
        Fout = W.shape[1]
        Wh = jnp.einsum('bnf,fo->bno', h, W)
        a1, a2 = (a[:Fout, 0], a[Fout:, 0])
        s1 = Wh @ a1
        s2 = Wh @ a2
        e = s1[:, :, None] + s2[:, None, :]
        e = jnp.where(e >= 0, e, ALPHA * e)
        e = jnp.where(adj_matrix[None] == 0, -jnp.inf, e)
        attention = jax.nn.softmax(e, axis=-1)
        h_prime = jnp.einsum('bij,bjo->bio', attention, Wh)
        return h_prime

    def _L3_gnn_ref(x, adj, Wg0, bg0, Wg1, bg1, Wih, Whh, bih, bhh):
        import jax, jax.numpy as jnp
        import numpy as np
        B, T, D, H = (64, 1024, 128, 128)
        MAX_SKIP = 4

        def _lstm_last(Wih, Whh, bih, bhh, xs):
            N, _, Hd = xs.shape
            bias = bih + bhh

            def step(carry, x_t):
                h, c = carry
                g = x_t @ Wih.T + h @ Whh.T + bias
                i, f, gg, o = jnp.split(g, 4, axis=-1)
                c = jax.nn.sigmoid(f) * c + jax.nn.sigmoid(i) * jnp.tanh(gg)
                h = jax.nn.sigmoid(o) * jnp.tanh(c)
                return ((h, c), None)
            init = (jnp.zeros((N, Hd), xs.dtype), jnp.zeros((N, Hd), xs.dtype))
            (h_last, _), _ = jax.lax.scan(step, init, jnp.swapaxes(xs, 0, 1))
            return h_last
        h = jax.nn.relu(jnp.einsum('ts,bsh->bth', adj, x @ Wg0 + bg0))
        h = jax.nn.relu(jnp.einsum('ts,bsh->bth', adj, h @ Wg1 + bg1))
        Bv, Tv, Hd = h.shape
        for p in range(1, MAX_SKIP + 1):
            nw = Tv // p
            wins = h[:, :nw * p, :].reshape(Bv * nw, p, Hd)
            last = _lstm_last(Wih[p - 1], Whh[p - 1], bih[p - 1], bhh[p - 1], wins)
            idx = jnp.arange(nw) * p + (p - 1)
            h = h.at[:, idx, :].set(last.reshape(Bv, nw, Hd))
        return h
    x = _layernorm(x + _L0_gnn_ref(x, adj, adj, L0_gnn_bias_in, L0_gnn_bias_out, L0_gnn_gate_w_in, L0_gnn_gate_b_in, L0_gnn_gate_w_out, L0_gnn_gate_b_out, L0_gnn_loop_gate), axis=-1)
    x = _layernorm(x + _L1_gnn_ref(x, adj, L1_gnn_W1, L1_gnn_b1, L1_gnn_g1, L1_gnn_be1, L1_gnn_W2, L1_gnn_b2, L1_gnn_g2, L1_gnn_be2), axis=-1)
    x = _layernorm(x + _L2_gnn_ref(x, adj, L2_gnn_W, L2_gnn_a), axis=-1)
    x = _layernorm(x + _L3_gnn_ref(x, adj, L3_gnn_Wg0, L3_gnn_bg0, L3_gnn_Wg1, L3_gnn_bg1, L3_gnn_Wih, L3_gnn_Whh, L3_gnn_bih, L3_gnn_bhh), axis=-1)
    return x

_drawn_inputs = setup_inputs


def setup_inputs(seed=0):
    import zlib

    import numpy as np

    out = dict(_drawn_inputs(seed))
    spreads = {'L0_gnn_gate_b_in': (0.0, 0.8),
     'L0_gnn_gate_b_out': (0.0, 0.8),
     'L1_gnn_b1': (0.0, 0.8),
     'L1_gnn_g1': (1.0, 0.2),
     'L1_gnn_be1': (0.0, 0.1),
     'L1_gnn_b2': (0.0, 0.8),
     'L1_gnn_g2': (1.0, 0.2),
     'L1_gnn_be2': (0.0, 0.1),
     'L3_gnn_bg0': (0.0, 0.8),
     'L3_gnn_bg1': (0.0, 0.8)}
    factors = {'L0_gnn_bias_in': 8.0,
     'L0_gnn_bias_out': 8.0,
     'L0_gnn_gate_w_in': 4.631,
     'L0_gnn_gate_w_out': 5.154,
     'L0_gnn_loop_gate': 3.483,
     'L3_gnn_Wg0': 8.0,
     'L3_gnn_Wg1': 8.0,
     'L3_gnn_Wih': 7.008,
     'L3_gnn_Whh': 8.0,
     'L3_gnn_bih': 2.851,
     'L3_gnn_bhh': 2.907}
    for name, (base, spread) in spreads.items():
        noise = np.random.default_rng([zlib.crc32(name.encode()), seed]).standard_normal(out[name].shape)
        drawn = base * np.exp(spread * noise) if base else spread * noise
        out[name] = jnp.asarray(drawn.astype(out[name].dtype))
    for name, factor in factors.items():
        out[name] = (out[name] * factor).astype(out[name].dtype)
    return out
```

```python
from contextlib import ExitStack

import concourse.bass as bass
import numpy as np
from concourse import mybir
from concourse.alu_op_type import AluOpType as ALU

F32 = mybir.dt.float32
ACT = mybir.ActivationFunctionType
AX = mybir.AxisListType

P = 128
BATCH, NODES, FEAT = 32, 256, 128
NC = NODES // P
GB = 4
GROUPS = BATCH // GB
TILES = NC * GB
COLS = GB * NODES
HID = 256
HC = HID // P
BANK = 512
SKIPS = 4
EPS = 1e-5
SLOPE = 0.2
MASKED = -1e30
PADT = NODES + 2

STEPS = [(1, 0, 0, 2, 256), (1, 0, 2, 2, 256)]
for _p in range(2, SKIPS + 1):
    STEPS += [(_p, _s, 0, GB, -(-NODES // _p)) for _s in range(_p)]
NSTEP = len(STEPS)
I, F, G, O = range(4)


def gates_of(k):
    return [I, G, O] if STEPS[k][1] == 0 else [I, G, F, O]


GATE_AT = {}
for _k in range(NSTEP):
    for _q in gates_of(_k):
        GATE_AT[_k, _q] = len(GATE_AT)
NGATE = len(GATE_AT)
FORGETS = [sum(STEPS[j][1] > 0 for j in range(k)) for k in range(NSTEP + 1)]
LAST_BEFORE = {p: max(k for k in range(NSTEP) if STEPS[k][0] < p) for p in range(2, SKIPS + 1)}

ROWS = {}
_at = 0
for _name, _n in (("bih", 16), ("bhh", 16), ("b1", 2), ("g1", 2), ("be1", 2), ("b2", 1), ("g2", 1),
                  ("be2", 1), ("gate_in", 1), ("gate_out", 1), ("gate_loop", 1), ("a1", 1), ("a2", 1),
                  ("gb_in", 2), ("gb_out", 2)):
    ROWS[_name] = (_at, _n)
    _at += _n
NROWS = _at


def build(nc, x, adj, bias_in, bias_out, gate_w_in, gate_b_in, gate_w_out, gate_b_out, loop_gate,
          W1, b1, g1, be1, W2, b2, g2, be2, W, a, Wg0, bg0, Wg1, bg1, Wih, Whh, bih, bhh, out):
    ctx = ExitStack()
    with ctx:
        def sb(name, shape):
            return ctx.enter_context(nc.sbuf_tensor(name, [P] + shape, F32))

        def sem(name):
            return ctx.enter_context(nc.semaphore(name))

        def reach(eng, s, n):
            if isinstance(n, int) and n <= 0:
                return
            eng.wait_ge(s, n)

        X1 = sb("X1", [GROUPS, TILES * P])
        HB = sb("HB", [HC, GROUPS * COLS])
        O2T = HB[:, 0, :]
        late = HB[:, 1, :].rearrange("p (k n) -> p k n", k=4)
        MS, E1, E2 = (late[:, k, :].rearrange("p (t n) -> p t n", n=NODES) for k in range(3))
        PT = MS
        HS = late[:, 3, 0:2 * BANK].rearrange("p (k n) -> p k n", k=2)
        ZF = late[:, 3, 2 * BANK:4 * BANK]
        AN, ANT = (late[:, 0, k * BANK:(k + 1) * BANK].rearrange("p (c n) -> p c n", c=NC) for k in range(2))
        W1R = late[:, 1, 0:HID].rearrange("p (c d) -> p c d", c=HC)
        W2R = late[:, 1, HID:2 * HID]
        WTR = late[:, 1, BANK:BANK + P]
        AR = late[:, 1, 2 * BANK:2 * BANK + P + 1]
        rows = late[:, 1, 3 * BANK:3 * BANK + P]
        DGS = late[:, 2, 0:P]
        two_a = sb("two_a", [2, TILES * P])
        XIN = X3 = two_a
        two_b = sb("two_b", [2, TILES * P])
        X1S = OUT = two_b
        one_a = sb("one_a", [COLS])
        XT0 = X2T = one_a
        one_b = sb("one_b", [COLS])
        AG = X3T = one_b
        one_c = sb("one_c", [COLS])
        U = YT = one_c
        one_d = sb("one_d", [COLS])
        V = H0T = one_d
        Z = sb("Z", [TILES * P])
        X2 = sb("X2", [TILES * P])
        Y = sb("Y", [TILES * P])
        V2 = Y
        WH = sb("WH", [TILES, P + 2])
        HT = sb("HT", [2, GB, PADT])
        raw = sb("raw", [2, SKIPS * 4, P])
        raw_f = raw[:].rearrange("p k t d -> p (k t d)").rearrange("p (k n) -> p k n", n=BANK)
        TG = [raw_f[:, q, :] for q in range(4)]
        TC, CA, CF, CELL = (raw_f[:, 4 + q, :] for q in range(4))
        WT = sb("WT", [2, SKIPS * 4, P])
        ident = sb("ident", [P])
        ADJ = sb("ADJ", [NC, NODES])
        ADJT = sb("ADJT", [NC, NODES])
        AHT = sb("AHT", [NC, NODES])
        NEG = sb("NEG", [NC, NODES])
        W1T = sb("W1T", [HID])
        W2T = sb("W2T", [HC, P])
        WX = sb("WX", [P + 1])
        WA2 = sb("WA2", [P])
        WG = sb("WG", [2, P])
        BGB = sb("BGB", [2, P])
        BIO = sb("BIO", [2, NC, P])
        GBI = sb("GBI", [NC, GB, 4])
        cols = sb("cols", [NROWS])
        GW = sb("GW", [4])
        BL = sb("BL", [SKIPS, 4])
        deg = sb("deg", [4, NC])
        dinv = sb("dinv", [NC])
        pw = sb("pw", [8])
        GZ = sb("GZ", [TILES, 4])
        GT = sb("GT", [TILES, 4])
        GG = sb("GG", [TILES, 4])
        GS = sb("GS", [TILES])
        ST1 = sb("ST1", [HC, GROUPS * 2, 6])
        ST2 = sb("ST2", [GROUPS * 2, 6])
        BN = sb("BN", [8, HC])
        BNM = sb("BNM", [HC, 2])
        STL = [sb(f"STL{k}", [TILES, 6]) for k in range(2)]
        SUM = [sb(f"SUM{k}", [TILES, 2]) for k in range(2)]
        DIF = [sb(f"DIF{k}", [TILES]) for k in range(2)]
        SQD = [sb(f"SQD{k}", [TILES]) for k in range(2)]
        MEAN = [sb(f"MEAN{k}", [TILES]) for k in range(2)]
        VAR = [sb(f"VAR{k}", [TILES]) for k in range(2)]
        RSD = [sb(f"RSD{k}", [TILES]) for k in range(2)]
        MX = sb("MX", [TILES])
        ZM = sb("ZM", [TILES])
        MM = sb("MM", [TILES])
        EB = sb("EB", [2, TILES])
        RD = sb("RD", [TILES])

        PA = ctx.enter_context(nc.psum_tensor("PA", [P, 2 * BANK], F32))
        PB = ctx.enter_context(nc.psum_tensor("PB", [P, 2 * BANK], F32))
        Q = [ctx.enter_context(nc.psum_tensor(f"Q{k}", [P, BANK], F32)) for k in range(4)]
        AB = [PA[:, 0:BANK], PA[:, BANK:], PB[:, 0:BANK], PB[:, BANK:]]

        (adj_in, w_in, lstm_in, x_in0, x_in1, sent0, sent1,
         ident0, ident_ok, exponent_ok, zero_ok, masks_ok, cleared) = (sem(n) for n in (
             "adj_in", "w_in", "lstm_in", "x_in0", "x_in1", "sent0", "sent1", "ident0", "ident_ok", "exponent_ok", "zero_ok", "masks_ok", "cleared"))
        x_in = [x_in0, x_in1]
        sent = [sent0, sent1]
        KEPT = 16 * GROUPS // 2
        setup_pe, setup_dve, setup_step, deg_ok, dinv_ok = (
            sem(n) for n in ("setup_pe", "setup_dve", "setup_step", "deg_ok", "dinv_ok"))
        lstm_turn, lstm_wt = sem("lstm_turn"), sem("lstm_wt")
        xt_ps, xt_ok, gate_ps, gate_z, gate_t, gate_g, gate_s = (
            sem(n) for n in ("xt_ps", "xt_ok", "gate_ps", "gate_z", "gate_t", "gate_g", "gate_s"))
        agg0_ps, loop_ok, bias_a, bias_b, bias_ok, mix1, mix2, mix3 = (
            sem(n) for n in ("agg0_ps", "loop_ok", "bias_a", "bias_b", "bias_ok", "mix1", "mix2", "mix3"))
        ln = [{s: sem(f"ln{k}_{s}") for s in ("stats", "sum", "dif", "sqd", "mean", "m2", "var", "rstd", "out")} for k in range(4)]
        agg1_ps, agg1_ok, hid_ps, hid_ok, hid_st = (
            sem(n) for n in ("agg1_ps", "agg1_ok", "hid_ps", "hid_ok", "hid_st"))
        bn_step, bn_var, bn_rstd, bn_ok = (sem(n) for n in ("bn_step", "bn_var", "bn_rstd", "bn_ok"))
        act_ok, out2_ps, out2_ok, out2_st = (sem(n) for n in ("act_ok", "out2_ps", "out2_ok", "out2_st"))
        (yt_ok, y_ps, z1_ok, x2t_ps, x2t_ok, s2_ps, wh_ps, wh_ok, max_ok, eb_a, eb_b, eb_ok, exps_ok,
         e_ok, et_ps, pt_ok, att_ps, rd_ok, z2_ok, x3t_ps, x3t_ok, y0_ps, y0_ok, h0_ps, h0_ok, y1_ps,
         y1_ok, h1_ps, h1_ok, ht_ps, zf_ok) = (sem(n) for n in (
             "yt_ok", "y_ps", "z1_ok", "x2t_ps", "x2t_ok", "s2_ps", "wh_ps", "wh_ok", "max_ok", "eb_a",
             "eb_b", "eb_ok", "exps_ok", "e_ok", "et_ps", "pt_ok", "att_ps", "rd_ok", "z2_ok", "x3t_ps",
             "x3t_ok", "y0_ps", "y0_ok", "h0_ps", "h0_ok", "y1_ps", "y1_ok", "h1_ps", "h1_ok", "ht_ps",
             "zf_ok"))
        max_due = sem("max_due")
        g_ps, g_ok, ca_ok, cf_ok, cell_ok, tc_ok, h_ok = (
            sem(n) for n in ("g_ps", "g_ok", "ca_ok", "cf_ok", "cell_ok", "tc_ok", "h_ok"))

        def tile(buf, c, b):
            t = c * GB + b
            return buf[:, t * P:(t + 1) * P]

        def turned(buf, c, b):
            at = b * NODES + c * P
            return buf[:, at:at + P]

        ORDER = [(c, b) for c in range(NC) for b in range(GB)]
        xg = x.rearrange("(g b) (c p) d -> g p c b d", b=GB, p=P)
        og = out.rearrange("(g b) (c p) d -> g p c b d", b=GB, p=P)

        def col(name, k=0, n=1):
            at = ROWS[name][0] + k
            return cols[:, at:at + n]

        def steps_view(buf, k):
            _, _, _, nb, nw = STEPS[k]
            return buf[:, 0:nb * nw].rearrange("p (b w) -> p b w", b=nb)

        def ht_view(par, k):
            p, s, b0, nb, nw = STEPS[k]
            return HT[:, par, b0:b0 + nb, s:s + (nw - 1) * p + 1:p]

        def pairs(run, first, count):
            assert count % 2 == 0
            return first, count // 2, run

        block = ctx.enter_context(nc.Block())

        @block.sync
        def _(sp):
            sp.dma_start(ADJ[:], adj.rearrange("(c p) m -> p c m", p=P)).then_inc(adj_in, 16)

            def load(g, par):
                reach(sp, mix3, g - 1)
                for c in range(NC):
                    sp.dma_start(XIN[:, par, c * BANK:(c + 1) * BANK].rearrange("p (b d) -> p b d", b=GB),
                                 xg[g, :, c]).then_inc(x_in[par], 16)

            def keep(g, par):
                sp.wait_ge(ln[0]["out"], TILES * (g + 1))
                sp.dma_start(X1[:, g, :], X1S[:, par]).then_inc(sent[par], 16)

            load(0, 0)
            for name, src in (("bih", bih), ("bhh", bhh)):
                at = ROWS[name][0]
                sp.dma_start(rows[at:at + 16, :], src.rearrange("k (q d) -> (k q) d", d=P)).then_inc(w_in, 16)
            for name, src in (("b1", b1), ("g1", g1), ("be1", be1), ("b2", b2), ("g2", g2), ("be2", be2)):
                at, n = ROWS[name]
                sp.dma_start(rows[at:at + n, :], src.rearrange("(q d) -> q d", d=P)).then_inc(w_in, 16)
            for name, src in (("gate_in", gate_w_in), ("gate_out", gate_w_out), ("gate_loop", loop_gate)):
                at = ROWS[name][0]
                sp.dma_start(rows[at:at + 1, :], src.rearrange("d q -> q d")).then_inc(w_in, 16)
            at = ROWS["a1"][0]
            sp.dma_start(rows[at:at + 2, :], a.rearrange("(k d) q -> k (d q)", d=P)).then_inc(w_in, 16)
            for name, src in (("gb_in", gate_b_in), ("gb_out", gate_b_out)):
                at = ROWS[name][0]
                sp.dma_start(rows[at:at + 2, :], src.rearrange("(k d) q -> k (d q)", d=P)).then_inc(w_in, 16)
            sp.dma_start(BIO[:, 0], bias_in.rearrange("(c p) d -> p c d", p=P)).then_inc(w_in, 16)
            sp.dma_start(BIO[:, 1], bias_out.rearrange("(c p) d -> p c d", p=P)).then_inc(w_in, 16)
            sp.dma_start(W1R, W1.rearrange("(c p) d -> p c d", p=P)).then_inc(w_in, 16)
            sp.dma_start(W2R, W2).then_inc(w_in, 16)
            sp.dma_start(WX[:, 0:P], W).then_inc(w_in, 16)
            sp.dma_start(WG[:, 0], Wg0).then_inc(w_in, 16)
            sp.dma_start(WG[:, 1], Wg1).then_inc(w_in, 16)
            sp.dma_start(BGB[:, 0], bg0.rearrange("(q d) -> q d", q=1).broadcast_to([P, P])).then_inc(w_in, 16)
            sp.dma_start(BGB[:, 1], bg1.rearrange("(q d) -> q d", q=1).broadcast_to([P, P])).then_inc(w_in, 16)
            load(1, 1)
            sp.dma_start(raw[:, 0], Wih.rearrange("k (q p) d -> p (k q) d", p=P)).then_inc(lstm_in, 16)
            sp.dma_start(raw[:, 1], Whh.rearrange("k (q p) d -> p (k q) d", p=P)).then_inc(lstm_in, 16)
            with sp.Fori(0, GROUPS // 2 - 1) as i:
                for par in range(2):
                    keep(i * 2 + par, par)
                    load(i * 2 + par + 2, par)
            keep(GROUPS - 2, 0)
            keep(GROUPS - 1, 1)

            def store(g, par):
                sp.wait_ge(ln[3]["out"], TILES * (g + 1))
                for c in range(NC):
                    sp.dma_start(og[g, :, c], OUT[:, par, c * BANK:(c + 1) * BANK].rearrange("p (b d) -> p b d", b=GB)
                                 ).then_inc(sent[par], 16)

            with sp.Fori(0, GROUPS // 2) as i:
                for par in range(2):
                    store(i * 2 + par, par)
            for par in range(2):
                sp.wait_ge(sent[par], KEPT + 16 * NC * GROUPS // 2)

        NW_IN = 23

        @block.gpsimd
        def _(pool):
            pool.memset(ident[:], 0.0).then_inc(ident0, 1)
            pool.wait_ge(ident0, 1)
            pool.affine_select(out=ident[:], in_=ident[:], compare_op=ALU.not_equal, fill=1.0, base=0,
                               pattern=[[-1, P]], channel_multiplier=1).then_inc(ident_ok, 1)
            pool.memset(pw[:], -0.5).then_inc(exponent_ok, 1)
            pool.memset(HT[:], 0.0).then_inc(cleared, 1)
            pool.wait_ge(exponent_ok, 1)
            pool.wait_ge(deg_ok, 2)
            pool.tensor_tensor(dinv[:], deg[:, 3, :], pw[:, 0:NC], ALU.pow).then_inc(dinv_ok, 1)

            def rstd(k, kk, g):
                pool.wait_ge(ln[k]["var"], g + 1)
                pool.tensor_tensor(RSD[kk][:], VAR[kk][:], pw[:], ALU.pow).then_inc(ln[k]["rstd"], 1)

            def block0(g):
                def wide(k):
                    return BIO[:, k].unsqueeze(2).broadcast_to([P, NC, GB, P])

                def gate(k):
                    return GG[:, :, k:k + 1].rearrange("p (c b) q -> p c b q", c=NC).broadcast_to([P, NC, GB, P])

                pool.wait_ge(gate_g, g + 1)
                reach(pool, mix2, g)
                v = V[:].rearrange("p (c b d) -> p c b d", c=NC, b=GB)
                v2 = V2[:].rearrange("p (c b d) -> p c b d", c=NC, b=GB)
                pool.tensor_tensor(v, wide(0), gate(0), ALU.mult).then_inc(bias_a, 1)
                pool.tensor_tensor(v2, wide(1), gate(1), ALU.mult).then_inc(bias_b, 1)
                pool.wait_ge(bias_a, g + 1)
                pool.wait_ge(bias_b, g + 1)
                pool.tensor_tensor(V[:], V[:], V2[:], ALU.add).then_inc(bias_ok, 1)
                rstd(0, 0, g)

            pool.wait_ge(w_in, 16 * NW_IN)
            block0(0)
            with pool.Fori(1, GROUPS) as g:
                block0(g)
            for k in range(2):
                pool.wait_ge(bn_var, k + 1)
                n = HC if k == 0 else 1
                pool.tensor_tensor(BN[:, 1 + 3 * k, 0:n], BN[:, 3 * k, 0:n], pw[:, 0:n], ALU.pow).then_inc(bn_rstd, 1)

            def slot(g, front, tail):
                if tail:
                    rstd(3, 1, g - 2)
                if front:
                    rstd(1, 0, g)
                    rstd(2, 0, g)

            slot(0, True, False)
            slot(1, True, False)
            with pool.Fori(1, GROUPS // 2) as i:
                for par in range(2):
                    slot(i * 2 + par, True, True)
            slot(GROUPS, False, True)
            slot(GROUPS + 1, False, True)

        @block.tensor
        def _(pe):
            pe.wait_ge(ident_ok, 1)
            pe.wait_ge(w_in, 16 * NW_IN)
            pe.wait_ge(adj_in, 16)
            for c in range(NC):
                for m in range(NC):
                    pe.transpose(PA[:, m * NODES + c * P:m * NODES + (c + 1) * P], ADJ[:, c, m * P:(m + 1) * P], ident[:])
            for c in range(HC):
                pe.transpose(PB[:, c * P:(c + 1) * P], W1R[:, c, :], ident[:])
                pe.transpose(PB[:, BANK + c * P:BANK + (c + 1) * P], W2R[:, c * P:(c + 1) * P], ident[:])
            pe.transpose(Q[0][:, 0:P], WX[:, 0:P], ident[:])
            pe.transpose(Q[1][:, 0:NROWS], rows[0:NROWS, :], ident[0:NROWS, 0:NROWS]).then_inc(setup_pe, 1)
            pe.wait_ge(setup_dve, 1)
            pe.matmul(Q[2][:, 0:P + 1], WTR, AR, start=True, stop=True).then_inc(setup_pe, 1)
            pe.wait_ge(setup_dve, 2)
            for c in range(NC):
                for m in range(NC):
                    mm = pe.transpose(PA[:, m * NODES + c * P:m * NODES + (c + 1) * P], AN[:, c, m * P:(m + 1) * P], ident[:])
            mm.then_inc(setup_pe, 1)
            pe.wait_ge(setup_dve, 3)

            def block0(g, par):
                pe.wait_ge(x_in[par], (g - par) * 16 + 32)
                reach(pe, agg1_ok, g - 1)
                for c, b in ORDER:
                    mm = pe.transpose(turned(PA, c, b), tile(XIN[:, par], c, b), ident[:])
                mm.then_inc(xt_ps, 1)
                reach(pe, mix1, TILES * g)
                for n in range(NC):
                    for m in range(NC):
                        mm = pe.matmul(PB[:, n * BANK:(n + 1) * BANK], ADJT[:, m, n * P:(n + 1) * P],
                                       XIN[:, par, m * BANK:(m + 1) * BANK], start=(m == 0), stop=(m == NC - 1))
                mm.then_inc(agg0_ps, 1)
                pe.wait_ge(xt_ok, g + 1)
                reach(pe, gate_z, g)
                for c, b in ORDER:
                    t = c * GB + b
                    mm = pe.matmul(Q[3][:, t * 4:t * 4 + 4], turned(XT0, c, b), GW[:], start=True, stop=True)
                mm.then_inc(gate_ps, 1)

            def block1(g, par):
                pe.wait_ge(ln[0]["out"], TILES * (g + 1))
                pe.wait_ge(xt_ok, min(g + 2, GROUPS) if isinstance(g, int) else g + 2)
                for b in range(GB):
                    for m in range(NC):
                        mm = pe.matmul(PA[:, b * NODES:(b + 1) * NODES], tile(X1S[:, par], m, b), AHT[:, m, :],
                                       start=(m == 0), stop=(m == NC - 1))
                mm.then_inc(agg1_ps, 1)
                pe.wait_ge(agg1_ok, g + 1)
                for r in range(4):
                    q, h = divmod(r, HC)
                    reach(pe, hid_ok, 4 * g + max(r - 1, 0))
                    pe.matmul(Q[r % 2][:], W1T[:, h * P:(h + 1) * P], AG[:, q * BANK:(q + 1) * BANK],
                              start=True, stop=True).then_inc(hid_ps, 1)

            block0(0, 0)
            block0(1, 1)
            block1(0, 0)
            with pe.Fori(1, GROUPS // 2) as i:
                for par in range(2):
                    block0(i * 2 + par, par)
                    block1(i * 2 + par - 1, 1 - par)
            block1(GROUPS - 1, 1)

            pe.wait_ge(lstm_in, 32)
            for k in range(2):
                for p in range(SKIPS):
                    r = k * SKIPS + p
                    if r >= 4:
                        pe.wait_ge(lstm_wt, r - 3)
                    for q in range(4):
                        mm = pe.transpose(AB[r % 4][:, q * P:(q + 1) * P], raw[:, k, p * 4 + q, :], ident[:])
                    mm.then_inc(lstm_turn, 1)
            pe.wait_ge(hid_ok, 4 * GROUPS)
            def output1(g):
                pe.wait_ge(act_ok, 2 * (g + 1))
                for q in range(2):
                    reach(pe, out2_ok, 2 * g)
                    for h in range(HC):
                        mm = pe.matmul(Q[q][:], W2T[:, h, :], HB[:, h, bass.ds(g * COLS + q * BANK, BANK)],
                                       start=(h == 0), stop=(h == HC - 1))
                    mm.then_inc(out2_ps, 1)

            output1(0)
            with pe.Fori(1, GROUPS) as g:
                output1(g)

            def a_residual(g, par):
                pe.wait_ge(yt_ok, g + 1)
                reach(pe, h1_ok, g)
                for c, b in ORDER:
                    mm = pe.transpose(tile(PA, c, b), turned(YT, c, b), ident[:])
                mm.then_inc(y_ps, 1)

            def a_turn(g, par):
                pe.wait_ge(ln[1]["out"], TILES * (g + 1))
                pe.wait_ge(z1_ok, g + 1)
                for c, b in ORDER:
                    mm = pe.transpose(turned(PA, c, b), tile(X2, c, b), ident[:])
                mm.then_inc(x2t_ps, 1)

            def a_scores(g, par):
                pe.wait_ge(x2t_ok, g + 1)
                reach(pe, y1_ok, g)
                for q in range(2):
                    mm = pe.matmul(PB[:, q * BANK:(q + 1) * BANK], WA2[:], X2T[:, q * BANK:(q + 1) * BANK],
                                   start=True, stop=True)
                mm.then_inc(s2_ps, 1)
                a_project(g, 0)

            def a_project(g, c):
                if c:
                    pe.wait_ge(wh_ok, NC * g + c)
                for b in range(GB):
                    mm = pe.matmul(PA[:, b * NODES:b * NODES + P + 1], turned(X2T, c, b), WX[:], start=True, stop=True)
                mm.then_inc(wh_ps, 1)

            def a_turn_e(g):
                pe.wait_ge(wh_ok, NC * (g + 1))
                pe.wait_ge(max_ok, TILES * (g + 1))
                for b in range(GB):
                    pe.wait_ge(e_ok, GB * g + b + 1)
                    for c in range(NC):
                        for m in range(NC):
                            at = m * NODES + c * P
                            mm = pe.transpose(AB[b][:, at:at + P], E1[:, c * GB + b, m * P:(m + 1) * P], ident[:])
                    mm.then_inc(et_ps, 1)

            def a_attend(g):
                for b in range(GB):
                    pe.wait_ge(pt_ok, GB * g + b + 1)
                    for c in range(NC):
                        for m in range(NC):
                            mm = pe.matmul(AB[b][:, c * NODES:c * NODES + P + 2],
                                           PT[:, 2 * b + m, c * P:(c + 1) * P], WH[:, m * GB + b, :],
                                           start=(m == 0), stop=(m == NC - 1))
                    mm.then_inc(att_ps, 1)

            def a_turn3(g, par):
                pe.wait_ge(ln[2]["out"], TILES * (g + 1))
                pe.wait_ge(z2_ok, TILES * (g + 1))
                for c, b in ORDER:
                    mm = pe.transpose(turned(PA, c, b), tile(X3[:, par], c, b), ident[:])
                mm.then_inc(x3t_ps, 1)

            def a_weigh(g, k):
                pe.wait_ge(x3t_ok if k == 0 else h0_ok, g + 1)
                if k == 1:
                    pe.wait_ge(y0_ok, g + 1)
                src = X3T if k == 0 else H0T
                for c, b in ORDER:
                    mm = pe.matmul(tile(PB, c, b), turned(src, c, b), WG[:, k, :], start=True, stop=True)
                mm.then_inc(y0_ps if k == 0 else y1_ps, 1)

            def a_spread(g, k):
                pe.wait_ge(y0_ok if k == 0 else y1_ok, g + 1)
                pe.wait_ge(x3t_ok if k == 0 else h0_ok, g + 1)
                for b in range(GB):
                    for m in range(NC):
                        mm = pe.matmul(PA[:, b * NODES:(b + 1) * NODES], tile(Y, m, b), ADJT[:, m, :],
                                       start=(m == 0), stop=(m == NC - 1))
                mm.then_inc(h0_ps if k == 0 else h1_ps, 1)

            def lstm_x(g, par, k):
                p, s, _, nb, nw = STEPS[k]
                if k == 0:
                    pe.wait_ge(h1_ok, g + 1)
                elif s == 0 and p > 1:
                    pe.wait_ge(h_ok, NSTEP * g + LAST_BEFORE[p] + 1)
                for q in gates_of(k):
                    before = max((j for (kk, qq), j in GATE_AT.items() if qq == q and kk < k), default=None)
                    last = max(j for (kk, qq), j in GATE_AT.items() if qq == q)
                    reach(pe, g_ok, NGATE * g + before + 1 if before is not None else NGATE * (g - 1) + last + 1)
                    mm = pe.matmul(Q[q][:, 0:nb * nw].rearrange("p (b w) -> p b w", b=nb), WT[:, 0, (p - 1) * 4 + q, :], ht_view(par, k),
                                   start=True, stop=(s == 0))
                    if s == 0:
                        mm.then_inc(g_ps, 1)

            def lstm_h(g, k):
                p, s, _, nb, nw = STEPS[k]
                if s == 0:
                    return
                pe.wait_ge(h_ok, NSTEP * g + k)
                for q in gates_of(k):
                    pe.matmul(Q[q][:, 0:nb * nw], WT[:, 1, (p - 1) * 4 + q, :], HS[:, (k - 1) % 2, 0:nb * nw],
                              start=False, stop=True).then_inc(g_ps, 1)

            def t_turn(g, par):
                pe.wait_ge(h_ok, NSTEP * (g + 1))
                if not isinstance(g, int) or g + 2 < GROUPS + 2:
                    reach(pe, y1_ok, g + 2 if not isinstance(g, int) else min(g + 2, GROUPS))
                for c, b in ORDER:
                    mm = pe.transpose(tile(PB, c, b), HT[:, par, b, c * P:(c + 1) * P], ident[:])
                mm.then_inc(ht_ps, 1)

            def slot(g, par, front, lstm, tail):
                run = [lambda: a_residual(g, par), lambda: a_turn(g, par), lambda: a_scores(g, par),
                       lambda: a_project(g, 1), lambda: a_turn_e(g), lambda: a_attend(g),
                       lambda: a_turn3(g, par), lambda: a_weigh(g, 0), lambda: a_spread(g, 0),
                       lambda: a_weigh(g, 1), lambda: a_spread(g, 1)]
                if tail:
                    t_turn(g - 2, par)
                for k in range(NSTEP):
                    if lstm:
                        lstm_x(g - 1, 1 - par, k)
                    if front:
                        if k == 2:
                            pe.wait_ge(zf_ok, g - 1) if tail else None
                        run[k]()
                    if lstm:
                        lstm_h(g - 1, k)

            pe.wait_ge(bn_ok, 2)
            pe.wait_ge(lstm_wt, 8)
            slot(0, 0, True, False, False)
            slot(1, 1, True, True, False)
            with pe.Fori(1, GROUPS // 2) as i:
                for par in range(2):
                    slot(i * 2 + par, par, True, True, True)
            slot(GROUPS, 0, False, True, True)
            slot(GROUPS + 1, 1, False, False, True)

        @block.scalar
        def _(act):
            act.wait_ge(setup_dve, 3)

            def block0(g, par):
                act.wait_ge(xt_ps, g + 1)
                reach(act, gate_ps, g)
                act.activation(XT0[:], PA[:], ACT.Copy).then_inc(xt_ok, 1)
                act.wait_ge(gate_z, g + 1)
                act.activation(GT[:], GZ[:], ACT.Tanh, scale=0.5).then_inc(gate_t, 1)
                act.wait_ge(gate_g, g + 1)
                reach(act, mix1, TILES * g)
                for c, b in ORDER:
                    t = c * GB + b
                    act.activation(tile(U, c, b), tile(XIN[:, par], c, b), ACT.Copy,
                                   scale=GG[:, t, 2:3]).then_inc(loop_ok, 1)

            def block1(g):
                act.wait_ge(agg1_ps, g + 1)
                reach(act, hid_ps, 4 * g)
                act.activation(AG[:], PA[:], ACT.Copy).then_inc(agg1_ok, 1)
                for r in range(4):
                    q, h = divmod(r, HC)
                    act.wait_ge(hid_ps, 4 * g + r + 1)
                    act.activation(HB[:, h, bass.ds(g * COLS + q * BANK, BANK)], Q[r % 2][:], ACT.Copy).then_inc(hid_ok, 1)

            block0(0, 0)
            block0(1, 1)
            block1(0)
            with act.Fori(1, GROUPS // 2) as i:
                for par in range(2):
                    block0(i * 2 + par, par)
                    block1(i * 2 + par - 1)
            block1(GROUPS - 1)

            act.wait_ge(bn_ok, 1)
            with act.Fori(0, GROUPS) as g:
                for h in range(HC):
                    v = HB[:, h, bass.ds(g * COLS, COLS)]
                    act.activation(v, v, ACT.Relu, bias=BN[:, 2, h:h + 1], scale=BN[:, 1, h:h + 1]).then_inc(act_ok, 1)

            def a_turned(g):
                act.wait_ge(x2t_ps, g + 1)
                reach(act, wh_ps, NC * g)
                act.activation(X2T[:], PA[:], ACT.Copy).then_inc(x2t_ok, 1)

            def a_projected(g, c):
                act.wait_ge(wh_ps, NC * g + c + 1)
                reach(act, att_ps, GB * g)
                reach(act, eb_ok, 2 * g)
                act.activation(WH[:, c * GB:(c + 1) * GB, 0:P + 1],
                               PA[:].rearrange("p (b n) -> p b n", b=GB)[:, :, 0:P + 1], ACT.Copy).then_inc(wh_ok, 1)

            def a_exps(g):
                act.wait_ge(eb_ok, 2 * (g + 1))
                reach(act, et_ps, GB * g)
                for b in range(GB):
                    for c in range(NC):
                        t = c * GB + b
                        act.activation(E1[:, t], MS[:, 2 * b + c], ACT.Exp, bias=EB[:, 0, t:t + 1])
                        e = act.activation(E2[:, t], MS[:, 2 * b + c], ACT.Exp, bias=EB[:, 1, t:t + 1], scale=SLOPE)
                    e.then_inc(exps_ok, 1)

            def a_turned3(g):
                act.wait_ge(x3t_ps, g + 1)
                reach(act, y0_ps, g)
                act.activation(X3T[:], PA[:], ACT.Copy).then_inc(x3t_ok, 1)

            def a_relu(g):
                act.wait_ge(h0_ps, g + 1)
                reach(act, y1_ps, g)
                act.activation(H0T[:], PA[:], ACT.Relu).then_inc(h0_ok, 1)

            def lstm(g, k):
                p, s, _, nb, nw = STEPS[k]
                n = nb * nw
                j = NSTEP * g + k
                for q in gates_of(k):
                    act.wait_ge(g_ps, NGATE * g + GATE_AT[k, q] + 1)
                    reach(act, h_ok, j)
                    act.activation(TG[q][:, 0:n], Q[q][:, 0:n], ACT.Tanh, scale=1.0 if q == G else 0.5,
                                   bias=BL[:, p - 1, q:q + 1]).then_inc(g_ok, 1)
                act.wait_ge(cell_ok, j + 1)
                act.activation(TC[:, 0:n], CELL[:, 0:n], ACT.Tanh, scale=0.5).then_inc(tc_ok, 1)

            def slot(g, front, lst, tail):
                run = {1: lambda: a_turned(g), 2: lambda: a_projected(g, 0), 3: lambda: a_projected(g, 1),
                       4: lambda: a_exps(g), 6: lambda: a_turned3(g), 8: lambda: a_relu(g)}
                for k in range(NSTEP):
                    if front and k in run:
                        run[k]()
                    if lst:
                        lstm(g - 1, k)

            act.wait_ge(bn_ok, 2)
            slot(0, True, False, False)
            slot(1, True, True, False)
            with act.Fori(1, GROUPS // 2) as i:
                for par in range(2):
                    slot(i * 2 + par, True, True, True)
            slot(GROUPS, False, True, True)

        @block.vector
        def _(dve):
            count = [0]

            def done(ins):
                count[0] += 1
                ins.then_inc(setup_step, 1)
                dve.wait_ge(setup_step, count[0])

            dve.memset(AR, 0.0).then_inc(zero_ok, 1)
            dve.memset(GBI[:], 0.0).then_inc(zero_ok, 1)
            dve.memset(GW[:], 0.0).then_inc(zero_ok, 1)
            dve.memset(WH[:], 1.0).then_inc(zero_ok, 1)
            dve.wait_ge(zero_ok, 4)
            dve.wait_ge(adj_in, 16)
            dve.wait_ge(w_in, 16 * NW_IN)
            dve.wait_ge(ident_ok, 1)
            dve.wait_ge(setup_pe, 1)
            done(dve.tensor_copy(cols[:], Q[1][:, 0:NROWS]))
            for k, name in enumerate(("gb_in", "gb_out")):
                done(dve.tensor_copy(GBI[:, :, :, k], col(name, 0, NC).unsqueeze(2).broadcast_to([P, NC, GB])))
            done(dve.tensor_copy(WTR, Q[0][:, 0:P]))
            done(dve.tensor_copy(AR[:, 0:1], col("a1")))
            done(dve.tensor_scalar(AR[:, 1:P + 1], AR[:, 1:P + 1], col("a2"), None, ALU.add))
            done(dve.tensor_copy(GW[:, 0:3], col("gate_in", 0, 3)))
            done(dve.tensor_copy(W1T[:], PB[:, 0:HID]))
            done(dve.tensor_copy(W2T[:].rearrange("p c d -> p (c d)"), PB[:, BANK:BANK + HID]))
            done(dve.tensor_copy(ADJT[:].rearrange("p c d -> p (c d)"), PA[:, 0:NC * NODES]))
            dve.tensor_scalar(AR[:, 0:1], AR[:, 0:1], 1.0, None, ALU.mult).then_inc(setup_dve, 1)
            done(dve.tensor_tensor(BL[:].rearrange("p k q -> p (k q)"), col("bih", 0, 16), col("bhh", 0, 16), ALU.add))
            done(dve.tensor_scalar(BL[:, :, 0:2], BL[:, :, 0:2], 0.5, None, ALU.mult))
            done(dve.tensor_scalar(BL[:, :, 3:4], BL[:, :, 3:4], 0.5, None, ALU.mult))
            dve.tensor_scalar(NEG[:], ADJ[:], 0.0, MASKED, ALU.is_equal, ALU.mult).then_inc(masks_ok, 1)
            done(dve.tensor_copy(AN, ADJ[:]))
            done(dve.tensor_copy(ANT, ADJT[:]))
            for c in range(NC):
                s = slice(c * P, (c + 1) * P)
                done(dve.tensor_tensor(AN[:, c, s], AN[:, c, s], ident[:], ALU.add))
                done(dve.tensor_tensor(ANT[:, c, s], ANT[:, c, s], ident[:], ALU.add))
                done(dve.tensor_tensor_reduce(DGS[:], AN[:, c, s], ident[:], 1.0, 0.0, ALU.mult, ALU.add, deg[:, 2, c:c + 1]))
            done(dve.tensor_reduce(deg[:, 0, :], AN, AX.X, ALU.add))
            done(dve.tensor_reduce(deg[:, 1, :], ANT, AX.X, ALU.add))
            dve.tensor_tensor(deg[:, 0, :], deg[:, 0, :], deg[:, 1, :], ALU.add).then_inc(deg_ok, 1)
            dve.wait_ge(deg_ok, 1)
            dve.tensor_tensor(deg[:, 3, :], deg[:, 0, :], deg[:, 2, :], ALU.subtract).then_inc(deg_ok, 1)
            dve.wait_ge(dinv_ok, 1)
            for c in range(NC):
                done(dve.tensor_scalar(AN[:, c, :], AN[:, c, :], dinv[:, c:c + 1], None, ALU.mult))
            dve.wait_ge(setup_pe, 2)
            done(dve.tensor_copy(WX[:, P:P + 1], Q[2][:, 0:1]))
            dve.tensor_copy(WA2[:], Q[2][:, 1:P + 1]).then_inc(setup_dve, 1)
            dve.wait_ge(setup_pe, 3)
            done(dve.tensor_scalar(AHT[:, 0, :], PA[:, 0:NODES], dinv[:, 0:1], None, ALU.mult))
            dve.tensor_scalar(AHT[:, 1, :], PA[:, NODES:2 * NODES], dinv[:, 1:2], None, ALU.mult).then_inc(setup_dve, 1)

            def norm_stats(k, kk, z, g):
                for t in range(TILES):
                    dve.bn_stats(STL[kk][:, t, :], z[:, t * P:(t + 1) * P]).then_inc(ln[k]["stats"], 1)
                dve.wait_ge(ln[k]["stats"], TILES * (g + 1))
                dve.tensor_tensor(SUM[kk][:], STL[kk][:, :, 1:3], STL[kk][:, :, 4:6], ALU.add).then_inc(ln[k]["sum"], 1)
                dve.tensor_tensor(DIF[kk][:], STL[kk][:, :, 1], STL[kk][:, :, 4], ALU.subtract).then_inc(ln[k]["dif"], 1)
                dve.wait_ge(ln[k]["dif"], g + 1)
                dve.tensor_tensor(SQD[kk][:], DIF[kk][:], DIF[kk][:], ALU.mult).then_inc(ln[k]["sqd"], 1)
                dve.wait_ge(ln[k]["sum"], g + 1)
                dve.tensor_scalar(MEAN[kk][:], SUM[kk][:, :, 0], 0.5, None, ALU.mult).then_inc(ln[k]["mean"], 1)
                dve.wait_ge(ln[k]["sqd"], g + 1)
                dve.scalar_tensor_tensor(out=SQD[kk][:], in0=SQD[kk][:], scalar=P / 4.0, in1=SUM[kk][:, :, 1],
                                         op0=ALU.mult, op1=ALU.add).then_inc(ln[k]["m2"], 1)
                dve.wait_ge(ln[k]["m2"], g + 1)
                dve.tensor_scalar(VAR[kk][:], SQD[kk][:], 1.0 / P, EPS, ALU.mult, ALU.add).then_inc(ln[k]["var"], 1)

            def norm_apply(k, kk, z, to, g):
                dve.wait_ge(ln[k]["rstd"], g + 1)
                for t in range(TILES):
                    dve.tensor_scalar(to[:, t * P:(t + 1) * P], z[:, t * P:(t + 1) * P], MEAN[kk][:, t:t + 1],
                                      RSD[kk][:, t:t + 1], ALU.subtract, ALU.mult).then_inc(ln[k]["out"], 1)

            def block0(g, par):
                dve.wait_ge(gate_ps, g + 1)
                dve.tensor_tensor(GZ[:].rearrange("p t q -> p (t q)"), Q[3][:, 0:TILES * 4],
                                  GBI[:].rearrange("p c b q -> p (c b q)"), ALU.add).then_inc(gate_z, 1)
                dve.wait_ge(gate_t, g + 1)
                reach(dve, loop_ok, TILES * g)
                reach(dve, bias_b, g)
                dve.tensor_scalar(GG[:], GT[:], 0.5, 0.5, ALU.mult, ALU.add).then_inc(gate_g, 1)
                dve.wait_ge(gate_g, g + 1)
                dve.tensor_tensor(GS[:], GG[:, :, 0], GG[:, :, 1], ALU.add).then_inc(gate_s, 1)
                dve.wait_ge(gate_s, g + 1)
                dve.wait_ge(agg0_ps, g + 1)
                for t in range(TILES):
                    dve.wait_ge(loop_ok, TILES * g + t + 1)
                    dve.scalar_tensor_tensor(out=Z[:, t * P:(t + 1) * P], in0=PB[:, t * P:(t + 1) * P], scalar=GS[:, t:t + 1],
                                             in1=U[:, t * P:(t + 1) * P], op0=ALU.mult, op1=ALU.add).then_inc(mix1, 1)
                dve.wait_ge(mix1, TILES * (g + 1))
                dve.wait_ge(bias_ok, g + 1)
                dve.tensor_tensor(Z[:], Z[:], V[:], ALU.add).then_inc(mix2, 1)
                dve.wait_ge(mix2, g + 1)
                dve.scalar_tensor_tensor(out=Z[:], in0=Z[:], scalar=0.0, in1=XIN[:, par], op0=ALU.max,
                                         op1=ALU.add).then_inc(mix3, 1)
                dve.wait_ge(mix3, g + 1)
                norm_stats(0, 0, Z, g)
                reach(dve, agg1_ps, g - 1)
                reach(dve, sent[par], (g - par) * 8)
                norm_apply(0, 0, Z, X1S[:, par], g)

            def block1(g):
                for r in range(4):
                    q, h = divmod(r, HC)
                    dve.wait_ge(hid_ok, 4 * g + r + 1)
                    dve.bn_stats(ST1[:, h, bass.ds(g * 2 + q, 1), :].rearrange("p a s -> p (a s)"), HB[:, h, bass.ds(g * COLS + q * BANK, BANK)]).then_inc(hid_st, 1)

            block0(0, 0)
            block0(1, 1)
            block1(0)
            with dve.Fori(1, GROUPS // 2) as i:
                for par in range(2):
                    block0(i * 2 + par, par)
                    block1(i * 2 + par - 1)
            block1(GROUPS - 1)

            step = [0]

            def then(ins):
                step[0] += 1
                ins.then_inc(bn_step, 1)
                dve.wait_ge(bn_step, step[0])

            def batch_norm(k, stats, n, bias, gamma, beta):
                var, rs, sh = BN[:, 3 * k, 0:n], BN[:, 3 * k + 1, 0:n], BN[:, 3 * k + 2, 0:n]
                mean = BN[:, 6, 0:n]
                for h in range(n):
                    then(dve.bn_aggr(BNM[:, h, :], stats[h]))
                then(dve.tensor_tensor(mean, BNM[:, 0:n, 0], bias, ALU.add))
                dve.tensor_scalar(var, BNM[:, 0:n, 1], EPS, None, ALU.add).then_inc(bn_var, 1)
                then(dve.tensor_tensor(sh, bias, mean, ALU.subtract))
                dve.wait_ge(bn_rstd, k + 1)
                then(dve.tensor_tensor(rs, rs, gamma, ALU.mult))
                then(dve.tensor_tensor(sh, sh, rs, ALU.mult))
                dve.tensor_tensor(sh, sh, beta, ALU.add).then_inc(bn_ok, 1)

            dve.wait_ge(hid_st, 4 * GROUPS)
            batch_norm(0, [ST1[:, h].rearrange("p a s -> p (a s)") for h in range(HC)], HC,
                       col("b1", 0, 2), col("g1", 0, 2), col("be1", 0, 2))
            for k in range(2):
                for p in range(SKIPS):
                    r = k * SKIPS + p
                    dve.wait_ge(lstm_turn, r + 1)
                    dve.tensor_scalar(WT[:, k, p * 4:(p + 1) * 4, :].rearrange("p q d -> p (q d)"), AB[r % 4], 0.5,
                                      None, ALU.mult).then_inc(lstm_wt, 1)
            with dve.Fori(0, GROUPS) as g:
                for q in range(2):
                    dve.wait_ge(out2_ps, 2 * g + 1 + q)
                    dve.tensor_copy(O2T[:, bass.ds(g * COLS + q * BANK, BANK)], Q[q][:]).then_inc(out2_ok, 1)
                for q in range(2):
                    dve.wait_ge(out2_ok, 2 * g + 1 + q)
                    dve.bn_stats(ST2[:, bass.ds(g * 2 + q, 1), :].rearrange("p a s -> p (a s)"), O2T[:, bass.ds(g * COLS + q * BANK, BANK)]).then_inc(out2_st, 1)
            dve.wait_ge(out2_st, 2 * GROUPS)
            batch_norm(1, [ST2[:].rearrange("p a s -> p (a s)")], 1, col("b2"), col("g2"), col("be2"))
            dve.wait_ge(bn_ok, 2)

            def a_scaled(g, par):
                reach(dve, y_ps, g)
                dve.tensor_scalar(YT[:], O2T[:, g * COLS:(g + 1) * COLS] if isinstance(g, int) else O2T[:, bass.ds(g * COLS, COLS)],
                                  BN[:, 4, 0:1], BN[:, 5, 0:1], ALU.mult, ALU.add).then_inc(yt_ok, 1)

            def a_sum1(g, par):
                dve.wait_ge(y_ps, g + 1)
                dve.tensor_tensor(Z[:], PA[:], X1[:, g, :], ALU.add).then_inc(z1_ok, 1)
                dve.wait_ge(z1_ok, g + 1)
                norm_stats(1, 0, Z, g)
                norm_apply(1, 0, Z, X2, g)

            def a_max(g):
                dve.wait_ge(s2_ps, g + 1)
                reach(dve, att_ps, GB * g)
                dve.memset(ZM[:], 0.0).then_inc(max_due, 1)
                for b in range(GB):
                    for c in range(NC):
                        t = c * GB + b
                        dve.tensor_tensor_reduce(MS[:, 2 * b + c], PB[:, b * NODES:(b + 1) * NODES], NEG[:, c], 1.0, -3e38,
                                                 ALU.add, ALU.max, MX[:, t:t + 1]).then_inc(max_ok, 1)

            def a_bias(g):
                s1 = WH[:, :, P]
                dve.wait_ge(wh_ok, NC * (g + 1))
                dve.wait_ge(max_ok, TILES * (g + 1))
                dve.wait_ge(max_due, g + 1)
                dve.tensor_tensor(ZM[:], MX[:], s1, ALU.add).then_inc(eb_a, 1)
                dve.wait_ge(eb_a, g + 1)
                dve.scalar_tensor_tensor(out=MM[:], in0=ZM[:], scalar=SLOPE, in1=ZM[:], op0=ALU.mult, op1=ALU.max).then_inc(eb_b, 1)
                dve.wait_ge(eb_b, g + 1)
                reach(dve, exps_ok, GB * g)
                dve.tensor_tensor(EB[:, 0], s1, MM[:], ALU.subtract).then_inc(eb_ok, 1)
                dve.scalar_tensor_tensor(out=EB[:, 1], in0=s1, scalar=SLOPE, in1=MM[:], op0=ALU.mult,
                                         op1=ALU.subtract).then_inc(eb_ok, 1)

            def a_weights(g):
                for b in range(GB):
                    dve.wait_ge(exps_ok, GB * g + b + 1)
                    dve.tensor_tensor(E1[:, b:TILES:GB], E1[:, b:TILES:GB], E2[:, b:TILES:GB], ALU.max).then_inc(e_ok, 1)
                for b in range(GB):
                    dve.wait_ge(et_ps, GB * g + b + 1)
                    dve.tensor_copy(PT[:, 2 * b:2 * b + 2].rearrange("p m n -> p (m n)"), AB[b]).then_inc(pt_ok, 1)

            def a_sum2(g, par):
                for b in range(GB):
                    dve.wait_ge(att_ps, GB * g + b + 1)
                    dve.reciprocal(RD[:, 2 * b:2 * b + 2], AB[b].rearrange("p (c n) -> p c n", c=NC)[:, :, P + 1]).then_inc(rd_ok, 1)
                    dve.wait_ge(rd_ok, GB * g + b + 1)
                    for c in range(NC):
                        dve.scalar_tensor_tensor(out=tile(Z, c, b), in0=AB[b][:, c * NODES:c * NODES + P],
                                                 scalar=RD[:, 2 * b + c:2 * b + c + 1], in1=tile(X2, c, b),
                                                 op0=ALU.mult, op1=ALU.add).then_inc(z2_ok, 1)
                dve.wait_ge(z2_ok, TILES * (g + 1))
                norm_stats(2, 0, Z, g)
                norm_apply(2, 0, Z, X3[:, par], g)

            def a_biased(g, k):
                dve.wait_ge(y0_ps if k == 0 else y1_ps, g + 1)
                if k == 0:
                    reach(dve, h1_ps, g)
                else:
                    dve.wait_ge(h0_ps, g + 1)
                dve.tensor_tensor(Y[:].rearrange("p (t d) -> p t d", d=P), PB[:].rearrange("p (t d) -> p t d", d=P),
                                  BGB[:, k:k + 1, :].broadcast_to([P, TILES, P]), ALU.add).then_inc(y0_ok if k == 0 else y1_ok, 1)

            def a_hidden(g, par):
                dve.wait_ge(h1_ps, g + 1)
                if isinstance(g, int) and g < 2:
                    dve.wait_ge(cleared, 1)
                reach(dve, ht_ps, g - 1)
                dve.tensor_scalar(HT[:, par, :, 0:NODES], PA[:].rearrange("p (b n) -> p b n", b=GB), 0.0, 2.0,
                                  ALU.max, ALU.mult).then_inc(h1_ok, 1)

            def lstm(g, par, k):
                p, s, _, nb, nw = STEPS[k]
                n = nb * nw
                j = NSTEP * g + k
                gate = NGATE * g
                dve.wait_ge(g_ok, gate + GATE_AT[k, G] + 1)
                target = CELL if s == 0 else CA
                reach(dve, tc_ok, j) if s == 0 else None
                dve.scalar_tensor_tensor(out=target[:, 0:n], in0=TG[I][:, 0:n], scalar=1.0, in1=TG[G][:, 0:n],
                                         op0=ALU.add, op1=ALU.mult).then_inc(cell_ok if s == 0 else ca_ok, 1)
                if s > 0:
                    f = FORGETS[NSTEP] * g + FORGETS[k] + 1
                    dve.wait_ge(g_ok, gate + GATE_AT[k, F] + 1)
                    dve.wait_ge(cell_ok, j)
                    dve.scalar_tensor_tensor(out=CF[:, 0:n], in0=TG[F][:, 0:n], scalar=1.0, in1=CELL[:, 0:n],
                                             op0=ALU.add, op1=ALU.mult).then_inc(cf_ok, 1)
                    dve.wait_ge(ca_ok, f)
                    dve.wait_ge(cf_ok, f)
                    dve.scalar_tensor_tensor(out=CELL[:, 0:n], in0=CF[:, 0:n], scalar=0.5, in1=CA[:, 0:n],
                                             op0=ALU.mult, op1=ALU.add).then_inc(cell_ok, 1)
                dve.wait_ge(g_ok, gate + GATE_AT[k, O] + 1)
                dve.wait_ge(tc_ok, j + 1)
                if s == p - 1:
                    to = ht_view(par, k)
                else:
                    to = steps_view(HS[:, k % 2], k)
                dve.scalar_tensor_tensor(out=to, in0=steps_view(TG[O], k), scalar=1.0, in1=steps_view(TC, k),
                                         op0=ALU.add, op1=ALU.mult).then_inc(h_ok, 1)

            def t_sum(g, par):
                dve.wait_ge(ht_ps, g + 1)
                dve.scalar_tensor_tensor(out=ZF[:], in0=PB[:], scalar=0.5, in1=X3[:, par], op0=ALU.mult,
                                         op1=ALU.add).then_inc(zf_ok, 1)
                dve.wait_ge(zf_ok, g + 1)
                norm_stats(3, 1, ZF, g)

            def t_norm(g, par):
                dve.wait_ge(sent[par], KEPT + (g - par) * 16)
                norm_apply(3, 1, ZF, OUT[:, par], g)

            def slot(g, par, front, lst, tail):
                run = [lambda: a_sum1(g, par), None, lambda: a_max(g), lambda: a_bias(g), lambda: a_weights(g),
                       lambda: a_sum2(g, par), None, lambda: a_biased(g, 0), None, lambda: a_biased(g, 1),
                       lambda: a_hidden(g, par)]
                if front:
                    a_scaled(g, par)
                if tail:
                    t_sum(g - 2, par)
                    t_norm(g - 2, par)
                for k in range(NSTEP):
                    if front and run[k]:
                        run[k]()
                    if lst:
                        lstm(g - 1, 1 - par, k)

            for par in range(2):
                dve.wait_ge(sent[par], KEPT)
            slot(0, 0, True, False, False)
            slot(1, 1, True, True, False)
            with dve.Fori(1, GROUPS // 2) as i:
                for par in range(2):
                    slot(i * 2 + par, par, True, True, True)
            slot(GROUPS, 0, False, True, True)
            slot(GROUPS + 1, 1, False, False, True)


_NAMES = ['x', 'adj', 'L0_gnn_bias_in', 'L0_gnn_bias_out', 'L0_gnn_gate_w_in', 'L0_gnn_gate_b_in',
          'L0_gnn_gate_w_out', 'L0_gnn_gate_b_out', 'L0_gnn_loop_gate', 'L1_gnn_W1', 'L1_gnn_b1', 'L1_gnn_g1',
          'L1_gnn_be1', 'L1_gnn_W2', 'L1_gnn_b2', 'L1_gnn_g2', 'L1_gnn_be2', 'L2_gnn_W', 'L2_gnn_a',
          'L3_gnn_Wg0', 'L3_gnn_bg0', 'L3_gnn_Wg1', 'L3_gnn_bg1', 'L3_gnn_Wih', 'L3_gnn_Whh', 'L3_gnn_bih',
          'L3_gnn_bhh']


def kernel(**inputs):
    import concourse.bacc as bacc
    from concourse.bass_utils import run_bass_kernel_spmd

    nc = bacc.Bacc("TRN2", target_bir_lowering=False, num_devices=1)
    arrays, args = {}, []
    for name in _NAMES:
        v = np.ascontiguousarray(inputs[name])
        arrays[f"in_{name}"] = v
        args.append(nc.dram_tensor(f"in_{name}", v.shape, mybir.dt.from_np(v.dtype), kind="ExternalInput").ap())
    args.append(nc.dram_tensor("out_0", (BATCH, NODES, FEAT), F32, kind="ExternalOutput").ap())
    build(nc, *args)
    r = run_bass_kernel_spmd(nc, [arrays], core_ids=[0])
    return r.results[0]["out_0"]
```
